# Optimizing a Trainium2 kernel written in Bass

```python
import numpy as np
import jax
import jax.numpy as jnp

def _softmax(x, axis=-1):
    return jax.nn.softmax(x, axis=axis)
def _gelu(x):
    return jax.nn.gelu(x, approximate=True)
def _silu(x):
    return jax.nn.silu(x)
def _sigmoid(x):
    return jax.nn.sigmoid(x)
def _layernorm(x, axis=-1, eps=1e-5):
    m = jnp.mean(x, axis=axis, keepdims=True)
    v = jnp.var(x, axis=axis, keepdims=True)
    return (x - m) / jnp.sqrt(v + eps)
def _scatter_add(tgt, idx, src, axis=0):
    return tgt.at[idx].add(src)
def _segment_sum(src, seg, n):
    return jax.ops.segment_sum(src, seg, n)

kernel_name = 'mk_adj_resnorm_d1_adj_128_df9762'

def setup_inputs(seed: int = 0):
    np.random.seed(seed)
    _w = jnp.asarray
    def _rec_inputs():
        import jax
        import jax.numpy as jnp
        _gk = jax.random.key(seed)
        x = -0.000929 + 1 * jax.random.normal(jax.random.fold_in(_gk, 1), (8192, 128), jnp.float32)
        _w = (1.0 + jnp.arange(8192, dtype=jnp.float32)) ** -0.5
        _w = _w / _w.mean()
        _pij = jnp.clip(0.00195312 * _w[:, None] * _w[None, :], 0.0, 1.0)
        _a = jax.random.uniform(jax.random.fold_in(_gk, 2), (8192, 8192)) < _pij
        adj = _a.astype(jnp.int32)
        return x, adj
    x, adj = _rec_inputs()
    def _L0_gnn_setup():
        import jax, jax.numpy as jnp
        import numpy as np
        NEG_BIG = -9000000000000000.0
        LEAKY_SLOPE = 0.2
        key = jax.random.key(seed)
        k1, k2, k3 = jax.random.split(key, 3)
        N, M, D = (8192, 8192, 128)
        qs = jax.random.normal(k1, (N, D), dtype=jnp.float32)
        ks = jax.random.normal(k2, (M, D), dtype=jnp.float32)
        HpGraph_e_k = jax.random.randint(k3, (N, M), 0, 2, dtype=jnp.int32)
        return {'qs': qs, 'ks': ks, 'HpGraph_e_k': HpGraph_e_k}
    _L0_gnn_all = _L0_gnn_setup()
    _L0_gnn_in = {k: v for k, v in _L0_gnn_all.items() if k in ('ks', )}
    del _L0_gnn_all

    return {
        "x": x,
        "adj": adj,
        "L0_gnn_ks": _L0_gnn_in["ks"],
    }

def reference(x, adj, L0_gnn_ks):
    import jax
    import jax.numpy as jnp
    def _L0_gnn_ref(qs, ks, HpGraph_e_k):
        import jax, jax.numpy as jnp
        import numpy as np
        NEG_BIG = -9000000000000000.0
        LEAKY_SLOPE = 0.2
        scores = jnp.einsum('nd,md->nm', qs, ks)
        scores = jax.nn.leaky_relu(scores, negative_slope=LEAKY_SLOPE)
        scores = jnp.where(HpGraph_e_k > 0, scores, NEG_BIG)
        attn = jax.nn.softmax(scores, axis=1)
        return jnp.einsum('nm,md->nd', attn, ks)

    x = _layernorm(x + _L0_gnn_ref(x, L0_gnn_ks, adj), axis=-1)
    return x


_drawn_inputs = setup_inputs


def setup_inputs(seed=0):
    import zlib

    import numpy as np

    out = dict(_drawn_inputs(seed))
    spreads = {}
    factors = {}
    for name, (base, spread) in spreads.items():
        noise = np.random.default_rng([zlib.crc32(name.encode()), seed]).standard_normal(out[name].shape)
        drawn = base * np.exp(spread * noise) if base else spread * noise
        out[name] = jnp.asarray(drawn.astype(out[name].dtype))
    for name, factor in factors.items():
        out[name] = (out[name] * factor).astype(out[name].dtype)
    return out
```

```python
import concourse.bass as bass
from concourse import mybir
from contextlib import ExitStack

F32 = mybir.dt.float32
F16 = mybir.dt.float16
BF16 = mybir.dt.bfloat16
I32 = mybir.dt.int32
ALU = mybir.AluOpType
ACT = mybir.ActivationFunctionType
AX = mybir.AxisListType

P = 128
SLOPE = 0.2
RISE = 1.0 / SLOPE - 1.0
EPS = 1e-5
MASKED = -(2.0 ** 120)
PROB_LIFT = 14 * 0.6931471805599453
TOP = 14
EXP_MASK = 0x7F800000
MANT = 1 << 23
MIN_EXP = 90


def adj_attention_layernorm(nc, x, x_t, ks, ks_t, adj, out):
    N, D = x.shape
    M = ks.shape[0]
    assert D == P
    TILES = N // P
    STEP = 1024
    HALF = 512
    STEPS = M // STEP
    HALVES = M // HALF
    PIECE = 2048
    PIECES = M // PIECE
    LOAD = 2048
    LOADS = M // LOAD
    BLOCKS = HALF // P
    PT_SLOTS = 4

    x_v = x.rearrange("(t p) d -> t p d", p=P)
    out_v = out.rearrange("(t p) d -> t p d", p=P)
    x_t_v = x_t.rearrange("d (t p) -> t d p", p=P)
    adj_v = adj.rearrange("(t p) (j m) -> t j p m", p=P, m=LOAD)
    ks_v = ks.rearrange("(b p) d -> p b d", p=P)

    ctx = ExitStack()
    with ctx:
        def sb(name, shape, dt):
            return ctx.enter_context(nc.sbuf_tensor(name, shape, dt))

        def ps(name, shape, dt):
            return ctx.enter_context(nc.psum_tensor(name, shape, dt))

        def sem(name):
            return ctx.enter_context(nc.semaphore(name))

        leaky = sb("leaky", [P, 2, M], F32)
        ks_t_raw = leaky[:, 0, :]
        x_t_raw = leaky[:, 1, :]
        ks_raw = leaky[:, 1, :]
        adj_sb = sb("adj_sb", [P, LOADS, LOAD], I32)
        bias = sb("bias", [P, 2, STEP], BF16)
        rise = sb("rise", [P, 2, STEP], F32)
        kt_hi = sb("kt_hi", [P, M], F16)
        kt_lo = sb("kt_lo", [P, M], F16)
        k_parts = sb("k_parts", [P, M // P, 2, D], F16)
        pt_hi = sb("pt_hi", [P, PT_SLOTS, HALF], F16)
        pt_lo = sb("pt_lo", [P, PT_SLOTS, HALF], F16)
        xt_raw = sb("xt_raw", [P, 2, P], F32)
        xt_scaled = sb("xt_scaled", [P, P], F32)
        xt_hi = sb("xt_hi", [P, 2, P], F16)
        xt_lo = sb("xt_lo", [P, 2, P], F16)
        x_row = sb("x_row", [P, 2, P], F32)
        eye32 = sb("eye32", [P, P], F32)
        eye16 = sb("eye16", [P, P], BF16)
        row_max = sb("row_max", [P, 2, STEPS], F32)
        exp_bias = sb("exp_bias", [P, 2], F32)
        sums = sb("sums", [P, 2, PIECES], F32)
        part = sb("part", [P, 2], F32)
        denom = sb("denom", [P, 2], F32)
        recip = sb("recip", [P, 1], F32)
        y0 = sb("y0", [P, P], F32)
        y = sb("y", [P, 2, P], F32)
        y_sum = sb("y_sum", [P, 2], F32)
        neg_mean = sb("neg_mean", [P, 1], F32)
        centred = sb("centred", [P, P], F32)
        squares = sb("squares", [P, P], F32)
        var = sb("var", [P, 1], F32)
        rstd = sb("rstd", [P, 1], F32)
        minus_half = sb("minus_half", [P, 1], F32)
        normed = sb("normed", [P, 2, P], F32)
        mag_k = sb("mag_k", [P, STEPS], F32)
        mag = sb("mag", [P, 2], F32)
        mag_all = sb("mag_all", [P, 2], F32)
        expo = sb("expo", [P, 2], I32)
        scale = sb("scale", [P, 2], I32)
        unscale = sb("unscale", [P, 2], I32)
        slope_scale = sb("slope_scale", [P, 2], F32)
        scale_x = scale[:, 0:1].bitcast(F32)
        scale_k = scale[:, 1:2].bitcast(F32)
        unscale_x = unscale[:, 0:1].bitcast(F32)
        unscale_k = unscale[:, 1:2].bitcast(F32)

        scores = ps("scores", [P, 2, STEP], F32)
        probs_t = ps("probs_t", [P, 2, HALF], F32)
        weighted = ps("weighted", [P, 2, HALF], F32)

        ks_t_loaded = [sem(f"ks_t_loaded{c}") for c in range(STEPS)]
        x_t_loaded = sem("x_t_loaded")
        ks_loaded = sem("ks_loaded")
        adj_loaded = [sem(f"adj_loaded{j}") for j in range(LOADS)]
        xt_loaded = [sem(f"xt_loaded{j}") for j in range(2)]
        xrow_loaded = [sem(f"xrow_loaded{j}") for j in range(2)]
        out_stored = [sem(f"out_stored{j}") for j in range(2)]
        const_step = sem("const_step")
        mag_x_ready = sem("mag_x_ready")
        mag_step = sem("mag_step")
        mag_all_ready = sem("mag_all_ready")
        scale_step = sem("scale_step")
        kt_hi_ready = sem("kt_hi_ready")
        kt_lo_ready = sem("kt_lo_ready")
        k_hi_ready = sem("k_hi_ready")
        k_lo_ready = sem("k_lo_ready")
        xt_step = sem("xt_step")
        bias_ready = sem("bias_ready")
        scores_ready = sem("scores_ready")
        rise_ready = sem("rise_ready")
        leaky_ready = sem("leaky_ready")
        exp_bias_ready = sem("exp_bias_ready")
        probs_ready = sem("probs_ready")
        probs_t_ready = sem("probs_t_ready")
        pt_hi_ready = sem("pt_hi_ready")
        pt_lo_ready = sem("pt_lo_ready")
        weighted_ready = sem("weighted_ready")
        denom_step = sem("denom_step")
        final_step = sem("final_step")
        norm_step = sem("norm_step")
        NORM_STEPS = 13

        block = ctx.enter_context(nc.Block())

        def wait(eng, semaphore, count):
            if not (isinstance(count, int) and count < 1):
                eng.wait_ge(semaphore, count)

        def detach(eng):
            eng.nop(nofuse=True)

        ROUNDS = TILES + 2

        def rounds(eng, one_round):
            for i in range(4):
                one_round(i, i % 2, i)
            with eng.Fori(4, TILES - 1, 2) as i:
                one_round(i, 0, None)
                one_round(i + 1, 1, None)
            for i in range(TILES, ROUNDS + 1):
                one_round(i, i % 2, i)

        def exists(peeled, back):
            return peeled is None or 0 <= peeled - back < TILES

        def in_slot(slot, first, every, count):
            for back in range(4):
                at = slot + HALVES * back - first
                if at >= 0 and at % every == 0 and at // every < count:
                    yield at // every, back

        @block.sync
        def _(sp):
            for c in range(STEPS):
                cols = slice(c * STEP, (c + 1) * STEP)
                sp.dma_start(ks_t_raw[:, cols], ks_t[:, cols]).then_inc(ks_t_loaded[c], 16)
            sp.dma_start(x_t_raw, x_t[:, :]).then_inc(x_t_loaded, 16)

            def load_tile(i, odd, peeled):
                if exists(peeled, 2):
                    wait(sp, final_step, 3 * (i - 3))
                    sp.dma_start(x_row[:, odd, :], x_v[i - 2, :, :]).then_inc(xrow_loaded[odd], 16)
                if exists(peeled, 0):
                    wait(sp, xt_step, 3 * (i - 1))
                    sp.dma_start(xt_raw[:, odd, :], x_t_v[i, :, :]).then_inc(xt_loaded[odd], 16)
                    for j in range(LOADS):
                        wait(sp, bias_ready, STEPS * (i - 1) + (j + 1) * LOAD // STEP)
                        sp.dma_start(adj_sb[:, j, :], adj_v[i, j, :, :]).then_inc(adj_loaded[j], 16)

            load_tile(0, 0, 0)
            sp.wait_ge(mag_x_ready, 1)
            sp.dma_start(ks_raw.rearrange("p (b d) -> p b d", d=D), ks_v).then_inc(ks_loaded, 16)
            for i in range(1, 4):
                load_tile(i, i % 2, i)
            with sp.Fori(4, TILES - 1, 2) as i:
                load_tile(i, 0, None)
                load_tile(i + 1, 1, None)
            load_tile(TILES, TILES % 2, TILES)
            load_tile(TILES + 1, (TILES + 1) % 2, TILES + 1)

        @block.gpsimd
        def _(pool):
            nc.gpsimd.memset(eye32[:, :], 0.0).then_inc(const_step, 1)
            nc.gpsimd.memset(eye16[:, :], 0.0).then_inc(const_step, 1)
            nc.gpsimd.memset(minus_half[:, :], -0.5).then_inc(const_step, 1)
            pool.wait_ge(const_step, 3)
            for n, eye in enumerate((eye32, eye16)):
                nc.gpsimd.affine_select(out=eye[:, :], in_=eye[:, :], compare_op=ALU.not_equal, fill=1.0,
                                        base=0, pattern=[[-1, P]], channel_multiplier=1).then_inc(const_step, 1)
            pool.wait_ge(mag_x_ready, 1)
            pool.wait_ge(mag_step, STEPS + 1)
            nc.gpsimd.partition_all_reduce(mag_all[:, :], mag[:, :], P, bass.bass_isa.ReduceOp.max)\
                .then_inc(mag_all_ready, 1)
            pool.wait_ge(scale_step, 6)

            def split_x(i, odd):
                pool.wait_ge(xt_loaded[odd], 8 * (i - odd) + 16)
                wait(pool, xt_step, 3 * i)
                detach(pool)
                nc.gpsimd.tensor_scalar(xt_scaled[:, :], xt_raw[:, odd, :], scale_x, 1.0, ALU.mult, ALU.mult)\
                    .then_inc(xt_step, 1)
                pool.wait_ge(xt_step, 3 * i + 1)
                wait(pool, scores_ready, STEPS * (i - 1))
                detach(pool)
                nc.gpsimd.tensor_copy(xt_hi[:, odd, :], xt_scaled[:, :]).then_inc(xt_step, 1)
                pool.wait_ge(xt_step, 3 * i + 2)
                nc.gpsimd.tensor_tensor(xt_lo[:, odd, :], xt_scaled[:, :], xt_hi[:, odd, :], ALU.subtract)\
                    .then_inc(xt_step, 1)

            def sum_probs(i, odd):
                pool.wait_ge(probs_ready, PIECES * (i + 1))
                wait(pool, final_step, 3 * (i - 1))
                nc.gpsimd.tensor_tensor(part[:, :], sums[:, odd, 0:2], sums[:, odd, 2:4], ALU.add)\
                    .then_inc(denom_step, 1)
                pool.wait_ge(denom_step, 3 * i + 1)
                nc.gpsimd.tensor_tensor(denom[:, odd:odd + 1], part[:, 0:1], part[:, 1:2], ALU.add)\
                    .then_inc(denom_step, 1)
                pool.wait_ge(denom_step, 3 * i + 2)
                detach(pool)
                nc.gpsimd.tensor_scalar(denom[:, odd:odd + 1], denom[:, odd:odd + 1], scale_k, 1.0,
                                        ALU.mult, ALU.mult).then_inc(denom_step, 1)

            def norm(i, odd):
                done = [0]

                def then(ins):
                    done[0] += 1
                    ins.then_inc(norm_step, 1)
                    pool.wait_ge(norm_step, NORM_STEPS * i + done[0])
                    detach(pool)

                pool.wait_ge(final_step, 3 * i + 3)
                detach(pool)
                then(nc.gpsimd.tensor_scalar(neg_mean[:, :], y_sum[:, odd:odd + 1], -1.0 / D, 1.0, ALU.mult, ALU.mult))
                then(nc.gpsimd.tensor_scalar(centred[:, :], y[:, odd, :], 1.0, neg_mean[:, :], ALU.mult, ALU.add))
                then(nc.gpsimd.tensor_tensor(squares[:, :], centred[:, :], centred[:, :], ALU.mult))
                width = D
                while width > 1:
                    width //= 2
                    then(nc.gpsimd.tensor_tensor(squares[:, 0:width], squares[:, 0:width],
                                                 squares[:, width:2 * width], ALU.add))
                then(nc.gpsimd.tensor_scalar(var[:, :], squares[:, 0:1], 1.0 / D, EPS, ALU.mult, ALU.add))
                then(nc.gpsimd.tensor_tensor(rstd[:, :], var[:, :], minus_half[:, :], ALU.pow))
                wait(pool, out_stored[odd], 8 * (i - odd))
                detach(pool)
                then(nc.gpsimd.tensor_scalar(normed[:, odd, :], centred[:, :], rstd[:, :], 1.0, ALU.mult, ALU.mult))
                assert done[0] == NORM_STEPS
                pool.dma_start(out_v[i, :, :], normed[:, odd, :]).then_inc(out_stored[odd], 16)

            split_x(0, 0)

            def one_round(i, odd, peeled):
                if exists(peeled, -1):
                    split_x(i + 1, 1 - odd)
                if exists(peeled, 2):
                    sum_probs(i - 2, odd)
                if exists(peeled, 3):
                    norm(i - 3, 1 - odd)

            for i in range(5):
                one_round(i, i % 2, i)
            with pool.Fori(5, TILES - 2, 2) as i:
                one_round(i, 1, None)
                one_round(i + 1, 0, None)
            for i in range(TILES - 1, TILES + 3):
                one_round(i, i % 2, i)
            for odd in range(2):
                pool.wait_ge(out_stored[odd], 16 * (TILES // 2))

        @block.scalar
        def _(act):
            act.wait_ge(x_t_loaded, 16)
            nc.scalar.activation(x_t_raw, x_t_raw, ACT.Abs, accum_out=mag[:, 0:1]).then_inc(mag_x_ready, 1)
            act.wait_ge(scale_step, 6)
            for c in range(STEPS):
                cols = slice(c * STEP, (c + 1) * STEP)
                nc.scalar.activation(kt_hi[:, cols], ks_t_raw[:, cols], ACT.Copy, scale=scale_k)\
                    .then_inc(kt_hi_ready, 1)

            def split_ks(c):
                rows = slice(c * STEP // P, (c + 1) * STEP // P)
                raw = ks_raw.rearrange("p (b d) -> p b d", d=D)
                act.wait_ge(ks_loaded, 16)
                nc.scalar.activation(k_parts[:, rows, 0, :], raw[:, rows, :], ACT.Copy, scale=scale_k)\
                    .then_inc(k_hi_ready, 1)

            def make_rise(t, c):
                act.wait_ge(scores_ready, STEPS * t + c + 1)
                wait(act, leaky_ready, STEPS * t + c - 1)
                nc.scalar.activation(rise[:, c % 2, :], scores[:, c % 2, :], ACT.Relu, scale=RISE)\
                    .then_inc(rise_ready, 1)

            def exponentials(t, odd, e):
                cols = slice(e * PIECE, (e + 1) * PIECE)
                act.wait_ge(exp_bias_ready, t + 1)
                if e == 0:
                    wait(act, denom_step, 3 * (t - 1))
                nc.scalar.activation(leaky[:, odd, cols], leaky[:, odd, cols], ACT.Exp,
                                     bias=exp_bias[:, odd:odd + 1], scale=slope_scale[:, 0:1],
                                     accum_out=sums[:, odd, e:e + 1]).then_inc(probs_ready, 1)

            def high_part(t, q):
                n = HALVES * t + q
                act.wait_ge(probs_t_ready, n + 1)
                wait(act, weighted_ready, n + 1 - PT_SLOTS)
                nc.scalar.activation(pt_hi[:, q % PT_SLOTS, :], probs_t[:, q % 2, :], ACT.Copy)\
                    .then_inc(pt_hi_ready, 1)

            def one_round(i, odd, peeled):
                for slot in range(HALVES):
                    if peeled == 0 and slot % 2 == 1:
                        split_ks(slot // 2)
                    for q, back in in_slot(slot, 23, 1, HALVES):
                        if exists(peeled, back):
                            high_part(i - back, q)
                    for c, back in in_slot(slot, 4, 2, STEPS):
                        if exists(peeled, back):
                            make_rise(i - back, c)
                    for e, back in in_slot(slot, 20, 4, PIECES):
                        if exists(peeled, back):
                            exponentials(i - back, (odd + back) % 2, e)

            rounds(act, one_round)

        @block.vector
        def _(dve):
            for c in range(STEPS):
                cols = slice(c * STEP, (c + 1) * STEP)
                dve.wait_ge(ks_t_loaded[c], 16)
                nc.vector.tensor_reduce(mag_k[:, c:c + 1], ks_t_raw[:, cols], AX.X, ALU.max,
                                        apply_absolute_value=True).then_inc(mag_step, 1)
            dve.wait_ge(mag_step, STEPS)
            nc.vector.tensor_reduce(mag[:, 1:2], mag_k[:, :], AX.X, ALU.max).then_inc(mag_step, 1)
            dve.wait_ge(mag_all_ready, 1)
            nc.vector.tensor_scalar(expo[:, :], mag_all[:, :].bitcast(I32), EXP_MASK, None, ALU.bitwise_and)\
                .then_inc(scale_step, 1)
            dve.wait_ge(scale_step, 1)
            nc.vector.tensor_scalar(expo[:, :], expo[:, :], float(MIN_EXP * MANT), None, ALU.max)\
                .then_inc(scale_step, 1)
            dve.wait_ge(scale_step, 2)
            nc.vector.tensor_scalar(scale[:, :], expo[:, :], -1.0, float((254 + TOP) * MANT), ALU.mult, ALU.add)\
                .then_inc(scale_step, 1)
            nc.vector.tensor_scalar(unscale[:, :], expo[:, :], -float(TOP * MANT), None, ALU.add)\
                .then_inc(scale_step, 1)
            dve.wait_ge(scale_step, 4)
            nc.vector.tensor_scalar(slope_scale[:, 0:1], unscale_x, unscale_k, SLOPE, ALU.mult, ALU.mult)\
                .then_inc(scale_step, 1)
            dve.wait_ge(scale_step, 5)
            nc.vector.tensor_scalar(slope_scale[:, 1:2], slope_scale[:, 0:1], -1.0, None, ALU.mult)\
                .then_inc(scale_step, 1)

            def split_ks_t(c):
                cols = slice(c * STEP, (c + 1) * STEP)
                dve.wait_ge(kt_hi_ready, c + 1)
                nc.vector.scalar_tensor_tensor(kt_lo[:, cols], ks_t_raw[:, cols], scale_k, kt_hi[:, cols],
                                               ALU.mult, ALU.subtract).then_inc(kt_lo_ready, 1)

            def split_ks(c):
                rows = slice(c * STEP // P, (c + 1) * STEP // P)
                raw = ks_raw.rearrange("p (b d) -> p b d", d=D)
                dve.wait_ge(k_hi_ready, c + 1)
                nc.vector.scalar_tensor_tensor(k_parts[:, rows, 1, :], raw[:, rows, :], scale_k,
                                               k_parts[:, rows, 0, :], ALU.mult, ALU.subtract)\
                    .then_inc(k_lo_ready, 1)

            def make_bias(t, c):
                j, at = c * STEP // LOAD, c * STEP % LOAD
                if at == 0:
                    dve.wait_ge(adj_loaded[j], 16 * (t + 1))
                wait(dve, scores_ready, STEPS * t + c - 1)
                nc.vector.tensor_scalar(bias[:, c % 2, :], adj_sb[:, j, at:at + STEP], 0.0, MASKED,
                                        ALU.is_le, ALU.mult).then_inc(bias_ready, 1)

            def make_leaky(t, odd, c, peeled):
                cols = slice(c * STEP, (c + 1) * STEP)
                dve.wait_ge(rise_ready, STEPS * t + c + 1)
                wait(dve, probs_t_ready, HALVES * (t - 2) + 2 * c + 2)
                if c == 0:
                    wait(dve, probs_ready, PIECES * (t - 1))
                    first = -3.0e38
                else:
                    dve.wait_ge(leaky_ready, STEPS * t + c)
                    first = row_max[:, odd, c - 1:c]
                if peeled is not None and t == 0:
                    dve.wait_ge(kt_lo_ready, c + 1)
                if peeled is not None and t == 1 and c == 0:
                    dve.wait_ge(k_lo_ready, STEPS)
                detach(dve)
                nc.vector.tensor_tensor_reduce(leaky[:, odd, cols], scores[:, c % 2, :], rise[:, c % 2, :],
                                               1.0, first, ALU.add, ALU.max, row_max[:, odd, c:c + 1])\
                    .then_inc(leaky_ready, 1)

            def make_exp_bias(t, odd):
                dve.wait_ge(leaky_ready, STEPS * (t + 1))
                nc.vector.tensor_scalar(exp_bias[:, odd:odd + 1], row_max[:, odd, STEPS - 1:STEPS],
                                        slope_scale[:, 1:2], PROB_LIFT, ALU.mult, ALU.add)\
                    .then_inc(exp_bias_ready, 1)

            def low_part(t, q):
                n = HALVES * t + q
                dve.wait_ge(pt_hi_ready, n + 1)
                nc.vector.tensor_tensor(pt_lo[:, q % PT_SLOTS, :], probs_t[:, q % 2, :],
                                        pt_hi[:, q % PT_SLOTS, :], ALU.subtract).then_inc(pt_lo_ready, 1)

            def finish(t, odd):
                dve.wait_ge(denom_step, 3 * t + 3)
                nc.vector.reciprocal(recip[:, :], denom[:, odd:odd + 1]).then_inc(final_step, 1)
                dve.wait_ge(weighted_ready, HALVES * (t + 1))
                dve.wait_ge(xrow_loaded[odd], 8 * (t - odd) + 16)
                dve.wait_ge(final_step, 3 * t + 1)
                nc.vector.scalar_tensor_tensor(y0[:, :], weighted[:, odd, 0:D], recip[:, :], x_row[:, odd, :],
                                               ALU.mult, ALU.add).then_inc(final_step, 1)
                dve.wait_ge(final_step, 3 * t + 2)
                wait(dve, norm_step, NORM_STEPS * (t - 1))
                nc.vector.scalar_tensor_tensor(y[:, odd, :], weighted[:, odd, D:2 * D], recip[:, :], y0[:, :],
                                               ALU.mult, ALU.add, accum_out=y_sum[:, odd:odd + 1])\
                    .then_inc(final_step, 1)

            def one_round(i, odd, peeled):
                for slot in range(HALVES):
                    for c, back in in_slot(slot, 0, 2, STEPS):
                        if exists(peeled, back):
                            make_bias(i - back, c)
                            if peeled == 0:
                                split_ks_t(c)
                    if peeled == 0 and slot % 2 == 1:
                        split_ks(slot // 2)
                    for c, back in in_slot(slot, 5, 2, STEPS):
                        if exists(peeled, back):
                            make_leaky(i - back, (odd + back) % 2, c, peeled)
                            if c == STEPS - 1:
                                make_exp_bias(i - back, (odd + back) % 2)
                    for q, back in in_slot(slot, 24, 1, HALVES):
                        if exists(peeled, back):
                            low_part(i - back, q)
                    for _, back in in_slot(slot, 42, 1, 1):
                        if exists(peeled, back):
                            finish(i - back, (odd + back) % 2)

            rounds(dve, one_round)

        @block.tensor
        def _(pe):
            pe.wait_ge(const_step, 5)

            def score(t, odd, c, h, peeled):
                cols = slice(c * STEP + h * HALF, c * STEP + (h + 1) * HALF)
                to = scores[:, c % 2, h * HALF:(h + 1) * HALF]
                if h == 0:
                    pe.wait_ge(bias_ready, STEPS * t + c + 1)
                    wait(pe, leaky_ready, STEPS * t + c - 1)
                    if c == 0:
                        pe.wait_ge(xt_step, 3 * t + 3)
                    if peeled is not None:
                        pe.wait_ge(kt_lo_ready, min(STEPS, STEPS * t + c + 1))
                nc.tensor.matmul(to, eye16[:, :], bias[:, c % 2, h * HALF:(h + 1) * HALF], start=True, stop=False)
                nc.tensor.matmul(to, xt_hi[:, odd, :], kt_hi[:, cols], start=False, stop=False)
                nc.tensor.matmul(to, xt_hi[:, odd, :], kt_lo[:, cols], start=False, stop=False)
                last = nc.tensor.matmul(to, xt_lo[:, odd, :], kt_hi[:, cols], start=False, stop=True)
                if h == 1:
                    last.then_inc(scores_ready, 1)

            def transpose(t, odd, q):
                n = HALVES * t + q
                if q * HALF % PIECE == 0:
                    pe.wait_ge(probs_ready, PIECES * t + q * HALF // PIECE + 1)
                wait(pe, pt_lo_ready, n - 1)
                for b in range(BLOCKS):
                    at = q * HALF + b * P
                    last = nc.tensor.transpose(probs_t[:, q % 2, b * P:(b + 1) * P],
                                               leaky[:, odd, at:at + P], eye32[:, :])
                last.then_inc(probs_t_ready, 1)

            def weigh(t, odd, q, peeled):
                slot = q % PT_SLOTS
                pe.wait_ge(pt_lo_ready, HALVES * t + q + 1)
                if q == 0:
                    wait(pe, final_step, 3 * (t - 1))
                if peeled is not None:
                    pe.wait_ge(k_lo_ready, STEPS)
                for b in range(BLOCKS):
                    rows = q * BLOCKS + b
                    cols = slice(b * P, (b + 1) * P)
                    nc.tensor.matmul(weighted[:, odd, 0:2 * D], pt_hi[:, slot, cols],
                                     k_parts[:, rows, :, :].rearrange("p a d -> p (a d)"),
                                     start=(rows == 0), stop=False, skip_group_check=True)
                    last = nc.tensor.matmul(weighted[:, odd, 0:D], pt_lo[:, slot, cols], k_parts[:, rows, 0, :],
                                            start=False, stop=(rows == M // P - 1), skip_group_check=True)
                last.then_inc(weighted_ready, 1)

            def one_round(i, odd, peeled):
                for slot in range(HALVES):
                    for n, back in in_slot(slot, 2, 1, HALVES):
                        if exists(peeled, back):
                            score(i - back, (odd + back) % 2, n // 2, n % 2, peeled)
                    for q, back in in_slot(slot, 23, 1, HALVES):
                        if exists(peeled, back):
                            transpose(i - back, (odd + back) % 2, q)
                    for q, back in in_slot(slot, 26, 1, HALVES):
                        if exists(peeled, back):
                            weigh(i - back, (odd + back) % 2, q, peeled)

            rounds(pe, one_round)


def kernel(x, adj, L0_gnn_ks):
    import numpy as np
    import concourse.bacc as bacc
    from concourse.bass_utils import run_bass_kernel_spmd

    x, adj, ks = np.asarray(x), np.asarray(adj), np.asarray(L0_gnn_ks)
    arrays = {
        "in_x": np.ascontiguousarray(x),
        "in_x_t": np.ascontiguousarray(x.T),
        "in_ks": np.ascontiguousarray(ks),
        "in_ks_t": np.ascontiguousarray(ks.T),
        "in_adj": np.ascontiguousarray(adj),
    }
    nc = bacc.Bacc("TRN2", target_bir_lowering=False, num_devices=1)
    args = [nc.dram_tensor(name, a.shape, mybir.dt.from_np(a.dtype), kind="ExternalInput").ap()
            for name, a in arrays.items()]
    out = nc.dram_tensor("out_0", x.shape, mybir.dt.float32, kind="ExternalOutput").ap()
    adj_attention_layernorm(nc, *args, out)
    r = run_bass_kernel_spmd(nc, [arrays], core_ids=[0])
    return r.results[0]["out_0"]
```

```python
import concourse.bass as bass
from concourse import mybir
from contextlib import ExitStack

F32 = mybir.dt.float32
F16 = mybir.dt.float16
BF16 = mybir.dt.bfloat16
I32 = mybir.dt.int32
ALU = mybir.AluOpType
ACT = mybir.ActivationFunctionType
AX = mybir.AxisListType

P = 128
SLOPE = 0.2
RISE = 1.0 / SLOPE - 1.0
EPS = 1e-5
MASKED = -(2.0 ** 120)
PROB_LIFT = 14 * 0.6931471805599453
TOP = 14
EXP_MASK = 0x7F800000
MANT = 1 << 23
MIN_EXP = 90


def adj_attention_layernorm(nc, x, x_t, ks, ks_t, adj, out):
    N, D = x.shape
    M = ks.shape[0]
    assert D == P
    TILES = N // P
    STEP = 1024
    HALF = 512
    STEPS = M // STEP
    HALVES = M // HALF
    PIECE = 1024
    PIECES = M // PIECE
    LOAD = 2048
    LOADS = M // LOAD
    BLOCKS = HALF // P
    PT_SLOTS = 4
    LOW, ONES, HIGH, WIDE = 0, D, D + 2, 2 * D + 2
    BANKS = 4
    BIASES = 4

    x_v = x.rearrange("(t p) d -> t p d", p=P)
    out_v = out.rearrange("(t p) d -> t p d", p=P)
    x_t_v = x_t.rearrange("d (t p) -> t d p", p=P)
    adj_v = adj.rearrange("(t p) (j m) -> t j p m", p=P, m=LOAD)
    ks_v = ks.rearrange("(b p) d -> p b d", p=P)

    ctx = ExitStack()
    with ctx:
        def sb(name, shape, dt):
            return ctx.enter_context(nc.sbuf_tensor(name, shape, dt))

        def ps(name, shape, dt):
            return ctx.enter_context(nc.psum_tensor(name, shape, dt))

        def sem(name):
            return ctx.enter_context(nc.semaphore(name))

        leaky = sb("leaky", [P, 2, M], F32)
        ks_t_raw = leaky[:, 0, :]
        x_t_raw = leaky[:, 1, :]
        ks_raw = leaky[:, 1, :]
        adj_sb = sb("adj_sb", [P, LOADS, LOAD], I32)
        bias = sb("bias", [P, BIASES, STEP], BF16)
        rise = sb("rise", [P, BANKS, HALF], F32)
        kt_hi = sb("kt_hi", [P, M], F16)
        kt_lo = sb("kt_lo", [P, M], F16)
        k_parts = sb("k_parts", [P, M // P, WIDE], F16)
        pt_hi = sb("pt_hi", [P, PT_SLOTS, HALF], F16)
        pt_lo = sb("pt_lo", [P, PT_SLOTS, HALF], F16)
        xt_raw = sb("xt_raw", [P, 2, P], F32)
        xt_scaled = sb("xt_scaled", [P, P], F32)
        xt_hi = sb("xt_hi", [P, 2, P], F16)
        xt_lo = sb("xt_lo", [P, 2, P], F16)
        x_row = sb("x_row", [P, 2, P], F32)
        eye = sb("eye", [P, P], F32)
        row_max = sb("row_max", [P, 2, HALVES], F32)
        exp_bias = sb("exp_bias", [P, 2], F32)
        denom = sb("denom", [P, 1], F32)
        recip = sb("recip", [P, 1], F32)
        y0 = sb("y0", [P, P], F32)
        y = sb("y", [P, 2, P], F32)
        y_sum = sb("y_sum", [P, 2], F32)
        neg_mean = sb("neg_mean", [P, 1], F32)
        squares = sb("squares", [P, P], F32)
        square_sum = sb("square_sum", [P, 1], F32)
        shift = sb("shift", [P, 1], F32)
        var = sb("var", [P, 1], F32)
        rstd = sb("rstd", [P, 1], F32)
        minus_half = sb("minus_half", [P, 1], F32)
        normed = sb("normed", [P, 2, P], F32)
        mag_x = sb("mag_x", [P, STEPS], F32)
        mag_k = sb("mag_k", [P, STEPS], F32)
        mag = sb("mag", [P, 2], F32)
        mag_all = sb("mag_all", [P, 2], F32)
        expo = sb("expo", [P, 2], I32)
        scale = sb("scale", [P, 2], I32)
        unscale = sb("unscale", [P, 2], I32)
        slope_scale = sb("slope_scale", [P, 2], F32)
        scale_x = scale[:, 0:1].bitcast(F32)
        scale_k = scale[:, 1:2].bitcast(F32)
        unscale_x = unscale[:, 0:1].bitcast(F32)
        unscale_k = unscale[:, 1:2].bitcast(F32)

        scores = ps("scores", [P, BANKS, HALF], F32)
        probs_t = ps("probs_t", [P, 2, HALF], F32)
        weighted = ps("weighted", [P, 2, HALF], F32)

        ks_t_loaded = [sem(f"ks_t_loaded{c}") for c in range(STEPS)]
        x_t_loaded = [sem(f"x_t_loaded{c}") for c in range(STEPS)]
        ks_loaded = sem("ks_loaded")
        adj_loaded = [sem(f"adj_loaded{j}") for j in range(LOADS)]
        xt_loaded = [sem(f"xt_loaded{j}") for j in range(2)]
        xrow_loaded = [sem(f"xrow_loaded{j}") for j in range(2)]
        out_stored = [sem(f"out_stored{j}") for j in range(2)]
        const_step = sem("const_step")
        mag_x_ready = sem("mag_x_ready")
        mag_step = sem("mag_step")
        mag_all_ready = sem("mag_all_ready")
        scale_step = sem("scale_step")
        kt_hi_ready = sem("kt_hi_ready")
        kt_lo_ready = sem("kt_lo_ready")
        k_hi_ready = sem("k_hi_ready")
        k_lo_ready = sem("k_lo_ready")
        xt_step = sem("xt_step")
        bias_ready = sem("bias_ready")
        scores_ready = sem("scores_ready")
        rise_ready = sem("rise_ready")
        masked_ready = sem("masked_ready")
        leaky_ready = sem("leaky_ready")
        exp_bias_ready = sem("exp_bias_ready")
        probs_ready = sem("probs_ready")
        probs_t_ready = sem("probs_t_ready")
        pt_hi_ready = sem("pt_hi_ready")
        pt_lo_ready = sem("pt_lo_ready")
        weighted_ready = sem("weighted_ready")
        final_step = sem("final_step")
        norm_step = sem("norm_step")
        NORM_STEPS = 6

        block = ctx.enter_context(nc.Block())

        def wait(eng, semaphore, count):
            if not (isinstance(count, int) and count < 1):
                eng.wait_ge(semaphore, count)

        def detach(eng):
            eng.nop(nofuse=True)

        AT_BIAS, AT_SCORE, AT_RISE, AT_MASK, AT_LEAKY = 0, 2, 3, 4, 5
        AT_EXP, AT_TRANSPOSE, AT_HIGH, AT_LOW, AT_WEIGH, AT_FINISH = 20, 23, 24, 24, 26, 42
        ROUNDS = TILES + 3

        def rounds(eng, one_round):
            for i in range(4):
                one_round(i, i % 2, i)
            with eng.Fori(4, TILES - 1, 2) as i:
                one_round(i, 0, None)
                one_round(i + 1, 1, None)
            for i in range(TILES, ROUNDS):
                one_round(i, i % 2, i)

        def exists(peeled, back):
            return peeled is None or 0 <= peeled - back < TILES

        def in_slot(slot, first, every, count):
            for back in range(4):
                at = slot + HALVES * back - first
                if at >= 0 and at % every == 0 and at // every < count:
                    yield at // every, back

        @block.sync
        def _(sp):
            for c in range(STEPS):
                cols = slice(c * STEP, (c + 1) * STEP)
                sp.dma_start(x_t_raw[:, cols], x_t[:, cols]).then_inc(x_t_loaded[c], 16)
                sp.dma_start(ks_t_raw[:, cols], ks_t[:, cols]).then_inc(ks_t_loaded[c], 16)

            def load_tile(i, odd, peeled):
                if exists(peeled, 2):
                    wait(sp, final_step, 4 * (i - 3))
                    sp.dma_start(x_row[:, odd, :], x_v[i - 2, :, :]).then_inc(xrow_loaded[odd], 16)
                if exists(peeled, 0):
                    wait(sp, xt_step, 3 * (i - 1))
                    sp.dma_start(xt_raw[:, odd, :], x_t_v[i, :, :]).then_inc(xt_loaded[odd], 16)
                    for j in range(LOADS):
                        if peeled == 0 and j == LOADS // 2:
                            sp.wait_ge(mag_x_ready, STEPS)
                            sp.dma_start(ks_raw.rearrange("p (b d) -> p b d", d=D), ks_v).then_inc(ks_loaded, 16)
                        wait(sp, bias_ready, STEPS * (i - 1) + (j + 1) * LOAD // STEP)
                        sp.dma_start(adj_sb[:, j, :], adj_v[i, j, :, :]).then_inc(adj_loaded[j], 16)

            for i in range(4):
                load_tile(i, i % 2, i)
            with sp.Fori(4, TILES - 1, 2) as i:
                load_tile(i, 0, None)
                load_tile(i + 1, 1, None)
            load_tile(TILES, TILES % 2, TILES)
            load_tile(TILES + 1, (TILES + 1) % 2, TILES + 1)

        @block.gpsimd
        def _(pool):
            nc.gpsimd.memset(eye[:, :], 0.0).then_inc(const_step, 1)
            nc.gpsimd.memset(minus_half[:, :], -0.5).then_inc(const_step, 1)
            nc.gpsimd.memset(k_parts[:, :, ONES:ONES + 1], 1.0).then_inc(const_step, 1)
            nc.gpsimd.memset(k_parts[:, :, ONES + 1:HIGH], 0.0).then_inc(const_step, 1)
            pool.wait_ge(const_step, 4)
            nc.gpsimd.affine_select(out=eye[:, :], in_=eye[:, :], compare_op=ALU.not_equal, fill=1.0,
                                    base=0, pattern=[[-1, P]], channel_multiplier=1).then_inc(const_step, 1)
            pool.wait_ge(mag_step, STEPS + 2)
            nc.gpsimd.partition_all_reduce(mag_all[:, :], mag[:, :], P, bass.bass_isa.ReduceOp.max)\
                .then_inc(mag_all_ready, 1)
            pool.wait_ge(scale_step, 6)

            def split_x(i, odd):
                pool.wait_ge(xt_loaded[odd], 8 * (i - odd) + 16)
                wait(pool, xt_step, 3 * i)
                detach(pool)
                nc.gpsimd.tensor_scalar(xt_scaled[:, :], xt_raw[:, odd, :], scale_x, 1.0, ALU.mult, ALU.mult)\
                    .then_inc(xt_step, 1)
                pool.wait_ge(xt_step, 3 * i + 1)
                wait(pool, scores_ready, HALVES * (i - 1))
                detach(pool)
                nc.gpsimd.tensor_copy(xt_hi[:, odd, :], xt_scaled[:, :]).then_inc(xt_step, 1)
                pool.wait_ge(xt_step, 3 * i + 2)
                nc.gpsimd.tensor_tensor(xt_lo[:, odd, :], xt_scaled[:, :], xt_hi[:, odd, :], ALU.subtract)\
                    .then_inc(xt_step, 1)

            def mask(t, n):
                c = n // 2
                if n % 2 == 0:
                    pool.wait_ge(bias_ready, STEPS * t + c + 1)
                pool.wait_ge(rise_ready, HALVES * t + n + 1)
                at = n % 2 * HALF
                nc.gpsimd.tensor_tensor(rise[:, n % BANKS, :], rise[:, n % BANKS, :], bias[:, c % BIASES, at:at + HALF],
                                        ALU.add).then_inc(masked_ready, 1)

            def mean(t, odd):
                pool.wait_ge(final_step, 4 * (t + 1))
                wait(pool, norm_step, NORM_STEPS * t)
                detach(pool)
                nc.gpsimd.tensor_scalar(neg_mean[:, :], y_sum[:, odd:odd + 1], -1.0 / D, 1.0, ALU.mult, ALU.mult)\
                    .then_inc(norm_step, 1)

            def deviation(t):
                pool.wait_ge(norm_step, NORM_STEPS * t + 2)
                detach(pool)
                nc.gpsimd.tensor_scalar(var[:, :], square_sum[:, :], 1.0 / D, EPS, ALU.mult, ALU.add)\
                    .then_inc(norm_step, 1)
                pool.wait_ge(norm_step, NORM_STEPS * t + 3)
                nc.gpsimd.tensor_tensor(rstd[:, :], var[:, :], minus_half[:, :], ALU.pow).then_inc(norm_step, 1)
                pool.wait_ge(norm_step, NORM_STEPS * t + 4)
                nc.gpsimd.tensor_tensor(shift[:, :], neg_mean[:, :], rstd[:, :], ALU.mult).then_inc(norm_step, 1)

            def store(t, odd):
                pool.wait_ge(norm_step, NORM_STEPS * (t + 1))
                pool.dma_start(out_v[t, :, :], normed[:, odd, :]).then_inc(out_stored[odd], 16)

            split_x(0, 0)

            def one_round(i, odd, peeled):
                for slot in range(HALVES):
                    for n, back in in_slot(slot, AT_MASK, 1, HALVES):
                        if exists(peeled, back):
                            mask(i - back, n)
                    for _, back in in_slot(slot, AT_FINISH + 1, 1, 1):
                        if exists(peeled, back):
                            mean(i - back, (odd + back) % 2)
                    for _, back in in_slot(slot, AT_FINISH + 3, 1, 1):
                        if exists(peeled, back):
                            deviation(i - back)
                    for _, back in in_slot(slot, AT_FINISH + 6, 1, 1):
                        if exists(peeled, back):
                            store(i - back, (odd + back) % 2)
                    if slot == 9 and exists(peeled, -1):
                        split_x(i + 1, 1 - odd)

            for i in range(5):
                one_round(i, i % 2, i)
            with pool.Fori(5, TILES - 2, 2) as i:
                one_round(i, 1, None)
                one_round(i + 1, 0, None)
            for i in range(TILES - 1, TILES + 4):
                one_round(i, i % 2, i)
            for odd in range(2):
                pool.wait_ge(out_stored[odd], 16 * (TILES // 2))

        @block.scalar
        def _(act):
            for c in range(STEPS):
                cols = slice(c * STEP, (c + 1) * STEP)
                act.wait_ge(x_t_loaded[c], 16)
                nc.scalar.activation(x_t_raw[:, cols], x_t_raw[:, cols], ACT.Abs, accum_out=mag_x[:, c:c + 1])\
                    .then_inc(mag_x_ready, 1)
            act.wait_ge(scale_step, 6)
            for c in range(STEPS):
                cols = slice(c * STEP, (c + 1) * STEP)
                nc.scalar.activation(kt_hi[:, cols], ks_t_raw[:, cols], ACT.Copy, scale=scale_k)\
                    .then_inc(kt_hi_ready, 1)

            def split_ks(c):
                rows = slice(c * STEP // P, (c + 1) * STEP // P)
                raw = ks_raw.rearrange("p (b d) -> p b d", d=D)
                act.wait_ge(ks_loaded, 16)
                nc.scalar.activation(k_parts[:, rows, HIGH:WIDE], raw[:, rows, :], ACT.Copy, scale=scale_k)\
                    .then_inc(k_hi_ready, 1)

            def make_rise(t, n):
                act.wait_ge(scores_ready, HALVES * t + n + 1)
                nc.scalar.activation(rise[:, n % BANKS, :], scores[:, n % BANKS, :], ACT.Relu, scale=RISE)\
                    .then_inc(rise_ready, 1)

            def exponentials(t, odd, e):
                cols = slice(e * PIECE, (e + 1) * PIECE)
                act.wait_ge(exp_bias_ready, t + 1)
                nc.scalar.activation(leaky[:, odd, cols], leaky[:, odd, cols], ACT.Exp,
                                     bias=exp_bias[:, odd:odd + 1], scale=slope_scale[:, 0:1])\
                    .then_inc(probs_ready, 1)

            def high_part(t, q):
                n = HALVES * t + q
                act.wait_ge(probs_t_ready, n + 1)
                wait(act, weighted_ready, n + 1 - PT_SLOTS)
                nc.scalar.activation(pt_hi[:, q % PT_SLOTS, :], probs_t[:, q % 2, :], ACT.Copy)\
                    .then_inc(pt_hi_ready, 1)

            def squares_of(t, odd):
                act.wait_ge(norm_step, NORM_STEPS * t + 1)
                nc.scalar.activation(squares[:, :], y[:, odd, :], ACT.Square, bias=neg_mean[:, :],
                                     accum_out=square_sum[:, :]).then_inc(norm_step, 1)

            def normalise(t, odd):
                act.wait_ge(norm_step, NORM_STEPS * t + 5)
                wait(act, out_stored[odd], 8 * (t - odd))
                nc.scalar.activation(normed[:, odd, :], y[:, odd, :], ACT.Identity, bias=shift[:, :],
                                     scale=rstd[:, :]).then_inc(norm_step, 1)

            def one_round(i, odd, peeled):
                for slot in range(HALVES):
                    if peeled == 0 and slot >= HALVES - STEPS:
                        split_ks(slot - (HALVES - STEPS))
                    for _, back in in_slot(slot, AT_FINISH + 2, 1, 1):
                        if exists(peeled, back):
                            squares_of(i - back, (odd + back) % 2)
                    for _, back in in_slot(slot, AT_FINISH + 5, 1, 1):
                        if exists(peeled, back):
                            normalise(i - back, (odd + back) % 2)
                    for q, back in in_slot(slot, AT_HIGH, 1, HALVES):
                        if exists(peeled, back):
                            high_part(i - back, q)
                    for n, back in in_slot(slot, AT_RISE, 1, HALVES):
                        if exists(peeled, back):
                            make_rise(i - back, n)
                    for e, back in in_slot(slot, AT_EXP, PIECE // HALF, PIECES):
                        if exists(peeled, back):
                            exponentials(i - back, (odd + back) % 2, e)

            rounds(act, one_round)

        @block.vector
        def _(dve):
            for c in range(STEPS):
                cols = slice(c * STEP, (c + 1) * STEP)
                dve.wait_ge(ks_t_loaded[c], 16)
                nc.vector.tensor_reduce(mag_k[:, c:c + 1], ks_t_raw[:, cols], AX.X, ALU.max,
                                        apply_absolute_value=True).then_inc(mag_step, 1)
            dve.wait_ge(mag_step, STEPS)
            nc.vector.tensor_reduce(mag[:, 1:2], mag_k[:, :], AX.X, ALU.max).then_inc(mag_step, 1)
            dve.wait_ge(mag_x_ready, STEPS)
            nc.vector.tensor_reduce(mag[:, 0:1], mag_x[:, :], AX.X, ALU.max).then_inc(mag_step, 1)
            dve.wait_ge(mag_all_ready, 1)
            nc.vector.tensor_scalar(expo[:, :], mag_all[:, :].bitcast(I32), EXP_MASK, None, ALU.bitwise_and)\
                .then_inc(scale_step, 1)
            dve.wait_ge(scale_step, 1)
            nc.vector.tensor_scalar(expo[:, :], expo[:, :], float(MIN_EXP * MANT), None, ALU.max)\
                .then_inc(scale_step, 1)
            dve.wait_ge(scale_step, 2)
            nc.vector.tensor_scalar(scale[:, :], expo[:, :], -1.0, float((254 + TOP) * MANT), ALU.mult, ALU.add)\
                .then_inc(scale_step, 1)
            nc.vector.tensor_scalar(unscale[:, :], expo[:, :], -float(TOP * MANT), None, ALU.add)\
                .then_inc(scale_step, 1)
            dve.wait_ge(scale_step, 4)
            nc.vector.tensor_scalar(slope_scale[:, 0:1], unscale_x, unscale_k, SLOPE, ALU.mult, ALU.mult)\
                .then_inc(scale_step, 1)
            dve.wait_ge(scale_step, 5)
            nc.vector.tensor_scalar(slope_scale[:, 1:2], slope_scale[:, 0:1], -1.0, None, ALU.mult)\
                .then_inc(scale_step, 1)

            def split_ks_t(c):
                cols = slice(c * STEP, (c + 1) * STEP)
                dve.wait_ge(kt_hi_ready, c + 1)
                nc.vector.scalar_tensor_tensor(kt_lo[:, cols], ks_t_raw[:, cols], scale_k, kt_hi[:, cols],
                                               ALU.mult, ALU.subtract).then_inc(kt_lo_ready, 1)

            def split_ks(c):
                rows = slice(c * STEP // P, (c + 1) * STEP // P)
                raw = ks_raw.rearrange("p (b d) -> p b d", d=D)
                dve.wait_ge(k_hi_ready, c + 1)
                nc.vector.scalar_tensor_tensor(k_parts[:, rows, LOW:D], raw[:, rows, :], scale_k,
                                               k_parts[:, rows, HIGH:WIDE], ALU.mult, ALU.subtract)\
                    .then_inc(k_lo_ready, 1)

            def make_bias(t, c):
                j, at = c * STEP // LOAD, c * STEP % LOAD
                if at == 0:
                    dve.wait_ge(adj_loaded[j], 16 * (t + 1))
                wait(dve, masked_ready, HALVES * t + 2 * (c - BIASES + 1))
                nc.vector.tensor_scalar(bias[:, c % BIASES, :], adj_sb[:, j, at:at + STEP], 0.0, MASKED,
                                        ALU.is_le, ALU.mult).then_inc(bias_ready, 1)

            def make_leaky(t, odd, n, peeled):
                cols = slice(n * HALF, (n + 1) * HALF)
                dve.wait_ge(masked_ready, HALVES * t + n + 1)
                wait(dve, probs_t_ready, HALVES * (t - 2) + n + 1)
                if n == 0:
                    wait(dve, exp_bias_ready, t - 1)
                    first = -3.0e38
                else:
                    dve.wait_ge(leaky_ready, HALVES * t + n)
                    first = row_max[:, odd, n - 1:n]
                if peeled is not None and t == 0:
                    dve.wait_ge(kt_lo_ready, n // 2 + 1)
                if peeled is not None and t == 1 and n == 0:
                    dve.wait_ge(k_lo_ready, STEPS)
                detach(dve)
                nc.vector.tensor_tensor_reduce(leaky[:, odd, cols], scores[:, n % BANKS, :], rise[:, n % BANKS, :],
                                               1.0, first, ALU.add, ALU.max, row_max[:, odd, n:n + 1])\
                    .then_inc(leaky_ready, 1)

            def make_exp_bias(t, odd):
                dve.wait_ge(leaky_ready, HALVES * (t + 1))
                wait(dve, probs_ready, PIECES * (t - 1))
                nc.vector.tensor_scalar(exp_bias[:, odd:odd + 1], row_max[:, odd, HALVES - 1:HALVES],
                                        slope_scale[:, 1:2], PROB_LIFT, ALU.mult, ALU.add)\
                    .then_inc(exp_bias_ready, 1)

            def low_part(t, q):
                n = HALVES * t + q
                dve.wait_ge(pt_hi_ready, n + 1)
                nc.vector.tensor_tensor(pt_lo[:, q % PT_SLOTS, :], probs_t[:, q % 2, :],
                                        pt_hi[:, q % PT_SLOTS, :], ALU.subtract).then_inc(pt_lo_ready, 1)

            def finish(t, odd):
                dve.wait_ge(weighted_ready, HALVES * (t + 1))
                nc.vector.tensor_scalar(denom[:, :], weighted[:, odd, ONES:ONES + 1], scale_k, None, ALU.mult)\
                    .then_inc(final_step, 1)
                dve.wait_ge(final_step, 4 * t + 1)
                nc.vector.reciprocal(recip[:, :], denom[:, :]).then_inc(final_step, 1)
                dve.wait_ge(xrow_loaded[odd], 8 * (t - odd) + 16)
                dve.wait_ge(final_step, 4 * t + 2)
                nc.vector.scalar_tensor_tensor(y0[:, :], weighted[:, odd, LOW:D], recip[:, :], x_row[:, odd, :],
                                               ALU.mult, ALU.add).then_inc(final_step, 1)
                dve.wait_ge(final_step, 4 * t + 3)
                wait(dve, norm_step, NORM_STEPS * (t - 1))
                nc.vector.scalar_tensor_tensor(y[:, odd, :], weighted[:, odd, HIGH:WIDE], recip[:, :], y0[:, :],
                                               ALU.mult, ALU.add, accum_out=y_sum[:, odd:odd + 1])\
                    .then_inc(final_step, 1)

            def one_round(i, odd, peeled):
                for slot in range(HALVES):
                    for c, back in in_slot(slot, AT_BIAS, 2, STEPS):
                        if exists(peeled, back):
                            make_bias(i - back, c)
                            if peeled == 0:
                                split_ks_t(c)
                    if peeled == 0 and slot >= HALVES - STEPS:
                        split_ks(slot - (HALVES - STEPS))
                    for n, back in in_slot(slot, AT_LEAKY, 1, HALVES):
                        if exists(peeled, back):
                            make_leaky(i - back, (odd + back) % 2, n, peeled)
                            if n == HALVES - 1:
                                make_exp_bias(i - back, (odd + back) % 2)
                    for q, back in in_slot(slot, AT_LOW, 1, HALVES):
                        if exists(peeled, back):
                            low_part(i - back, q)
                    for _, back in in_slot(slot, AT_FINISH, 1, 1):
                        if exists(peeled, back):
                            finish(i - back, (odd + back) % 2)

            rounds(dve, one_round)

        @block.tensor
        def _(pe):
            pe.wait_ge(const_step, 5)

            def score(t, odd, n, peeled):
                c, cols = n // 2, slice(n * HALF, (n + 1) * HALF)
                to = scores[:, n % BANKS, :]
                wait(pe, leaky_ready, HALVES * t + n + 1 - BANKS)
                if n == 0:
                    pe.wait_ge(xt_step, 3 * t + 3)
                if peeled is not None:
                    pe.wait_ge(kt_lo_ready, min(STEPS, STEPS * t + c + 1))
                nc.tensor.matmul(to, xt_hi[:, odd, :], kt_hi[:, cols], start=True, stop=False)
                nc.tensor.matmul(to, xt_hi[:, odd, :], kt_lo[:, cols], start=False, stop=False)
                nc.tensor.matmul(to, xt_lo[:, odd, :], kt_hi[:, cols], start=False, stop=True)\
                    .then_inc(scores_ready, 1)

            def transpose(t, odd, q):
                n = HALVES * t + q
                if q * HALF % PIECE == 0:
                    pe.wait_ge(probs_ready, PIECES * t + q * HALF // PIECE + 1)
                wait(pe, pt_lo_ready, n - 1)
                for b in range(BLOCKS):
                    at = q * HALF + b * P
                    last = nc.tensor.transpose(probs_t[:, q % 2, b * P:(b + 1) * P],
                                               leaky[:, odd, at:at + P], eye[:, :])
                last.then_inc(probs_t_ready, 1)

            def weigh(t, odd, q, peeled):
                slot = q % PT_SLOTS
                pe.wait_ge(pt_lo_ready, HALVES * t + q + 1)
                if q == 0:
                    wait(pe, final_step, 4 * (t - 1))
                if peeled is not None:
                    pe.wait_ge(k_lo_ready, STEPS)
                for b in range(BLOCKS):
                    rows = q * BLOCKS + b
                    cols = slice(b * P, (b + 1) * P)
                    nc.tensor.matmul(weighted[:, odd, 0:WIDE], pt_hi[:, slot, cols], k_parts[:, rows, :],
                                     start=(rows == 0), stop=False, skip_group_check=True)
                    last = nc.tensor.matmul(weighted[:, odd, ONES:WIDE], pt_lo[:, slot, cols],
                                            k_parts[:, rows, ONES:WIDE], start=False,
                                            stop=(rows == M // P - 1), skip_group_check=True)
                last.then_inc(weighted_ready, 1)

            def one_round(i, odd, peeled):
                for slot in range(HALVES):
                    for n, back in in_slot(slot, AT_SCORE, 1, HALVES):
                        if exists(peeled, back):
                            score(i - back, (odd + back) % 2, n, peeled)
                    for q, back in in_slot(slot, AT_TRANSPOSE, 1, HALVES):
                        if exists(peeled, back):
                            transpose(i - back, (odd + back) % 2, q)
                    for q, back in in_slot(slot, AT_WEIGH, 1, HALVES):
                        if exists(peeled, back):
                            weigh(i - back, (odd + back) % 2, q, peeled)

            rounds(pe, one_round)


def kernel(x, adj, L0_gnn_ks):
    import numpy as np
    import concourse.bacc as bacc
    from concourse.bass_utils import run_bass_kernel_spmd

    x, adj, ks = np.asarray(x), np.asarray(adj), np.asarray(L0_gnn_ks)
    arrays = {
        "in_x": np.ascontiguousarray(x),
        "in_x_t": np.ascontiguousarray(x.T),
        "in_ks": np.ascontiguousarray(ks),
        "in_ks_t": np.ascontiguousarray(ks.T),
        "in_adj": np.ascontiguousarray(adj),
    }
    nc = bacc.Bacc("TRN2", target_bir_lowering=False, num_devices=1)
    args = [nc.dram_tensor(name, a.shape, mybir.dt.from_np(a.dtype), kind="ExternalInput").ap()
            for name, a in arrays.items()]
    out = nc.dram_tensor("out_0", x.shape, mybir.dt.float32, kind="ExternalOutput").ap()
    adj_attention_layernorm(nc, *args, out)
    r = run_bass_kernel_spmd(nc, [arrays], core_ids=[0])
    return r.results[0]["out_0"]
```

```python
import concourse.bass as bass
from concourse import mybir
from contextlib import ExitStack

F32 = mybir.dt.float32
F16 = mybir.dt.float16
BF16 = mybir.dt.bfloat16
I32 = mybir.dt.int32
ALU = mybir.AluOpType
ACT = mybir.ActivationFunctionType
AX = mybir.AxisListType

P = 128
SLOPE = 0.2
RISE = 1.0 / SLOPE - 1.0
EPS = 1e-5
MASKED = -(2.0 ** 120)
PROB_LIFT = 14 * 0.6931471805599453
TOP = 14
EXP_MASK = 0x7F800000
MANT = 1 << 23
MIN_EXP = 90


def adj_attention_layernorm(nc, x, x_t, ks, ks_t, adj, out):
    N, D = x.shape
    M = ks.shape[0]
    assert D == P
    TILES = N // P
    STEP = 1024
    HALF = 512
    STEPS = M // STEP
    HALVES = M // HALF
    PIECE = 1024
    PIECES = M // PIECE
    LOAD = 2048
    LOADS = M // LOAD
    BLOCKS = HALF // P
    PT_SLOTS = 4
    LOW, ONES, HIGH, WIDE = 0, D, D + 2, 2 * D + 2
    BANKS = 4
    KS_SLOTS = 4
    EARLY = 4
    BIASES = 4

    x_v = x.rearrange("(t p) d -> t p d", p=P)
    out_v = out.rearrange("(t p) d -> t p d", p=P)
    x_t_v = x_t.rearrange("d (t p) -> t d p", p=P)
    adj_v = adj.rearrange("(t p) (j m) -> t j p m", p=P, m=LOAD)
    ks_v = ks.rearrange("(c b p) d -> c p b d", p=P, b=STEP // P)

    ctx = ExitStack()
    with ctx:
        def sb(name, shape, dt):
            return ctx.enter_context(nc.sbuf_tensor(name, shape, dt))

        def ps(name, shape, dt):
            return ctx.enter_context(nc.psum_tensor(name, shape, dt))

        def sem(name):
            return ctx.enter_context(nc.semaphore(name))

        leaky = sb("leaky", [P, 2, M], F32)
        ks_t_raw = leaky[:, 0, :]
        x_t_raw = leaky[:, 1, :]
        ks_raw = sb("ks_raw", [P, KS_SLOTS, STEP // D, D], F32)
        adj_sb = sb("adj_sb", [P, LOADS, LOAD], I32)
        bias = sb("bias", [P, BIASES, STEP], BF16)
        rise = sb("rise", [P, BANKS, HALF], F32)
        kt_hi = sb("kt_hi", [P, M], F16)
        kt_lo = sb("kt_lo", [P, M], F16)
        k_parts = sb("k_parts", [P, M // P, WIDE], F16)
        pt_hi = sb("pt_hi", [P, PT_SLOTS, HALF], F16)
        pt_lo = sb("pt_lo", [P, PT_SLOTS, HALF], F16)
        xt_raw = sb("xt_raw", [P, 2, P], F32)
        xt_scaled = sb("xt_scaled", [P, P], F32)
        xt_hi = sb("xt_hi", [P, 2, P], F16)
        xt_lo = sb("xt_lo", [P, 2, P], F16)
        x_row = sb("x_row", [P, 2, P], F32)
        eye = sb("eye", [P, P], F32)
        row_max = sb("row_max", [P, 2, HALVES], F32)
        exp_bias = sb("exp_bias", [P, 2], F32)
        denom = sb("denom", [P, 1], F32)
        recip = sb("recip", [P, 1], F32)
        y0 = sb("y0", [P, P], F32)
        y = sb("y", [P, 2, P], F32)
        y_sum = sb("y_sum", [P, 2], F32)
        neg_mean = sb("neg_mean", [P, 1], F32)
        squares = sb("squares", [P, P], BF16)
        square_sum = sb("square_sum", [P, 1], F32)
        shift = sb("shift", [P, 1], F32)
        var = sb("var", [P, 1], F32)
        rstd = sb("rstd", [P, 1], F32)
        minus_half = sb("minus_half", [P, 1], F32)
        normed = sb("normed", [P, 2, P], F32)
        mag_x = sb("mag_x", [P, STEPS], F32)
        mag_k = sb("mag_k", [P, STEPS], F32)
        mag = sb("mag", [P, 2], F32)
        mag_all = sb("mag_all", [P, 2], F32)
        expo = sb("expo", [P, 2], I32)
        scale = sb("scale", [P, 2], I32)
        unscale = sb("unscale", [P, 2], I32)
        slope_scale = sb("slope_scale", [P, 2], F32)
        scale_x = scale[:, 0:1].bitcast(F32)
        scale_k = scale[:, 1:2].bitcast(F32)
        unscale_x = unscale[:, 0:1].bitcast(F32)
        unscale_k = unscale[:, 1:2].bitcast(F32)

        scores = ps("scores", [P, BANKS, HALF], F32)
        probs_t = ps("probs_t", [P, 2, HALF], F32)
        weighted = ps("weighted", [P, 2, HALF], F32)

        ks_t_loaded = [sem(f"ks_t_loaded{c}") for c in range(STEPS)]
        x_t_loaded = [sem(f"x_t_loaded{c}") for c in range(STEPS)]
        ks_loaded = [sem(f"ks_loaded{j}") for j in range(KS_SLOTS)]
        adj_loaded = [sem(f"adj_loaded{j}") for j in range(LOADS)]
        xt_loaded = [sem(f"xt_loaded{j}") for j in range(2)]
        xrow_loaded = [sem(f"xrow_loaded{j}") for j in range(2)]
        out_stored = [sem(f"out_stored{j}") for j in range(2)]
        const_step = sem("const_step")
        mag_x_ready = sem("mag_x_ready")
        mag_step = sem("mag_step")
        mag_all_ready = sem("mag_all_ready")
        scale_step = sem("scale_step")
        kt_hi_ready = sem("kt_hi_ready")
        kt_lo_ready = sem("kt_lo_ready")
        k_hi_ready = sem("k_hi_ready")
        k_lo_ready = sem("k_lo_ready")
        xt_step = sem("xt_step")
        bias_ready = sem("bias_ready")
        scores_ready = sem("scores_ready")
        rise_ready = sem("rise_ready")
        masked_ready = sem("masked_ready")
        leaky_ready = sem("leaky_ready")
        exp_bias_ready = sem("exp_bias_ready")
        probs_ready = sem("probs_ready")
        probs_t_ready = sem("probs_t_ready")
        pt_hi_ready = sem("pt_hi_ready")
        pt_lo_ready = sem("pt_lo_ready")
        weighted_ready = sem("weighted_ready")
        final_step = sem("final_step")
        norm_step = sem("norm_step")
        MAG_STEPS = STEPS + 1 + STEPS // 2 + 1
        SCALE_STEPS = 10
        NORM_STEPS = 6

        block = ctx.enter_context(nc.Block())

        def wait(eng, semaphore, count):
            if not (isinstance(count, int) and count < 1):
                eng.wait_ge(semaphore, count)

        def detach(eng):
            eng.nop(nofuse=True)

        AT_BIAS, AT_SCORE, AT_RISE, AT_MASK, AT_LEAKY = 0, 2, 3, 4, 5
        AT_EXP, AT_TRANSPOSE, AT_HIGH, AT_LOW, AT_WEIGH, AT_FINISH = 20, 23, 24, 24, 26, 42
        AT_SPLIT_KS_T, AT_SPLIT_KS = 3, 16
        ROUNDS = TILES + 3

        def rounds(eng, one_round):
            for i in range(4):
                one_round(i, i % 2, i)
            with eng.Fori(4, TILES - 1, 2) as i:
                one_round(i, 0, None)
                one_round(i + 1, 1, None)
            for i in range(TILES, ROUNDS):
                one_round(i, i % 2, i)

        def exists(peeled, back):
            return peeled is None or 0 <= peeled - back < TILES

        def in_slot(slot, first, every, count):
            for back in range(4):
                at = slot + HALVES * back - first
                if at >= 0 and at % every == 0 and at // every < count:
                    yield at // every, back

        @block.sync
        def _(sp):
            for c in range(STEPS):
                cols = slice(c * STEP, (c + 1) * STEP)
                sp.dma_start(ks_t_raw[:, cols], ks_t[:, cols]).then_inc(ks_t_loaded[c], 16)
            for c in range(STEPS):
                cols = slice(c * STEP, (c + 1) * STEP)
                sp.dma_start(x_t_raw[:, cols], x_t[:, cols]).then_inc(x_t_loaded[c], 16)

            def load_ks(first, end):
                for c in range(first, end):
                    wait(sp, k_lo_ready, c + 1 - KS_SLOTS)
                    sp.dma_start(ks_raw[:, c % KS_SLOTS, :, :], ks_v[c, :, :, :])\
                        .then_inc(ks_loaded[c % KS_SLOTS], 16)

            def load_tile(i, odd, peeled):
                if exists(peeled, 2):
                    wait(sp, final_step, 4 * (i - 3))
                    sp.dma_start(x_row[:, odd, :], x_v[i - 2, :, :]).then_inc(xrow_loaded[odd], 16)
                if exists(peeled, 0):
                    wait(sp, xt_step, 3 * (i - 1))
                    sp.dma_start(xt_raw[:, odd, :], x_t_v[i, :, :]).then_inc(xt_loaded[odd], 16)
                    for j in range(LOADS):
                        if peeled == 0 and j == LOADS // 2:
                            load_ks(0, KS_SLOTS)
                        if peeled == 1 and j >= LOADS // 2:
                            load_ks(KS_SLOTS + 2 * j - LOADS, KS_SLOTS + 2 * j - LOADS + 2)
                        wait(sp, bias_ready, STEPS * (i - 1) + (j + 1) * LOAD // STEP)
                        sp.dma_start(adj_sb[:, j, :], adj_v[i, j, :, :]).then_inc(adj_loaded[j], 16)

            for i in range(4):
                load_tile(i, i % 2, i)
            with sp.Fori(4, TILES - 1, 2) as i:
                load_tile(i, 0, None)
                load_tile(i + 1, 1, None)
            load_tile(TILES, TILES % 2, TILES)
            load_tile(TILES + 1, (TILES + 1) % 2, TILES + 1)

        @block.gpsimd
        def _(pool):
            nc.gpsimd.memset(eye[:, :], 0.0).then_inc(const_step, 1)
            nc.gpsimd.memset(minus_half[:, :], -0.5).then_inc(const_step, 1)
            nc.gpsimd.memset(k_parts[:, :, ONES:ONES + 1], 1.0).then_inc(const_step, 1)
            nc.gpsimd.memset(k_parts[:, :, ONES + 1:HIGH], 0.0).then_inc(const_step, 1)
            pool.wait_ge(const_step, 4)
            nc.gpsimd.affine_select(out=eye[:, :], in_=eye[:, :], compare_op=ALU.not_equal, fill=1.0,
                                    base=0, pattern=[[-1, P]], channel_multiplier=1).then_inc(const_step, 1)
            for column, count in ((1, STEPS + 1), (0, MAG_STEPS)):
                pool.wait_ge(mag_step, count)
                nc.gpsimd.partition_all_reduce(mag_all[:, column:column + 1], mag[:, column:column + 1], P,
                                               bass.bass_isa.ReduceOp.max).then_inc(mag_all_ready, 1)
            pool.wait_ge(scale_step, SCALE_STEPS)

            def split_x(i, odd):
                pool.wait_ge(xt_loaded[odd], 8 * (i - odd) + 16)
                wait(pool, xt_step, 3 * i)
                detach(pool)
                nc.gpsimd.tensor_scalar(xt_scaled[:, :], xt_raw[:, odd, :], scale_x, 1.0, ALU.mult, ALU.mult)\
                    .then_inc(xt_step, 1)
                pool.wait_ge(xt_step, 3 * i + 1)
                wait(pool, scores_ready, HALVES * (i - 1))
                detach(pool)
                nc.gpsimd.tensor_copy(xt_hi[:, odd, :], xt_scaled[:, :]).then_inc(xt_step, 1)
                pool.wait_ge(xt_step, 3 * i + 2)
                nc.gpsimd.tensor_tensor(xt_lo[:, odd, :], xt_scaled[:, :], xt_hi[:, odd, :], ALU.subtract)\
                    .then_inc(xt_step, 1)

            def mask(t, n):
                c = n // 2
                if n % 2 == 0:
                    pool.wait_ge(bias_ready, STEPS * t + c + 1)
                pool.wait_ge(rise_ready, HALVES * t + n + 1)
                at = n % 2 * HALF
                nc.gpsimd.tensor_tensor(rise[:, n % BANKS, :], rise[:, n % BANKS, :], bias[:, c % BIASES, at:at + HALF],
                                        ALU.add).then_inc(masked_ready, 1)

            def mean(t, odd):
                pool.wait_ge(final_step, 4 * (t + 1))
                wait(pool, norm_step, NORM_STEPS * t)
                detach(pool)
                nc.gpsimd.tensor_scalar(neg_mean[:, :], y_sum[:, odd:odd + 1], -1.0 / D, 1.0, ALU.mult, ALU.mult)\
                    .then_inc(norm_step, 1)

            def deviation(t):
                pool.wait_ge(norm_step, NORM_STEPS * t + 2)
                detach(pool)
                nc.gpsimd.tensor_scalar(var[:, :], square_sum[:, :], 1.0 / D, EPS, ALU.mult, ALU.add)\
                    .then_inc(norm_step, 1)
                pool.wait_ge(norm_step, NORM_STEPS * t + 3)
                nc.gpsimd.tensor_tensor(rstd[:, :], var[:, :], minus_half[:, :], ALU.pow).then_inc(norm_step, 1)
                pool.wait_ge(norm_step, NORM_STEPS * t + 4)
                nc.gpsimd.tensor_tensor(shift[:, :], neg_mean[:, :], rstd[:, :], ALU.mult).then_inc(norm_step, 1)

            def store(t, odd):
                pool.wait_ge(norm_step, NORM_STEPS * (t + 1))
                pool.dma_start(out_v[t, :, :], normed[:, odd, :]).then_inc(out_stored[odd], 16)

            split_x(0, 0)

            def one_round(i, odd, peeled):
                for slot in range(HALVES):
                    for n, back in in_slot(slot, AT_MASK, 1, HALVES):
                        if exists(peeled, back):
                            mask(i - back, n)
                    for _, back in in_slot(slot, AT_FINISH + 1, 1, 1):
                        if exists(peeled, back):
                            mean(i - back, (odd + back) % 2)
                    for _, back in in_slot(slot, AT_FINISH + 3, 1, 1):
                        if exists(peeled, back):
                            deviation(i - back)
                    for _, back in in_slot(slot, AT_FINISH + 6, 1, 1):
                        if exists(peeled, back):
                            store(i - back, (odd + back) % 2)
                    if slot == 9 and exists(peeled, -1):
                        split_x(i + 1, 1 - odd)

            for i in range(5):
                one_round(i, i % 2, i)
            with pool.Fori(5, TILES - 2, 2) as i:
                one_round(i, 1, None)
                one_round(i + 1, 0, None)
            for i in range(TILES - 1, TILES + 4):
                one_round(i, i % 2, i)
            for odd in range(2):
                pool.wait_ge(out_stored[odd], 16 * (TILES // 2))

        @block.scalar
        def _(act):
            def bound_x(c):
                cols = slice(c * STEP, (c + 1) * STEP)
                act.wait_ge(x_t_loaded[c], 16)
                nc.scalar.activation(x_t_raw[:, cols], x_t_raw[:, cols], ACT.Abs, accum_out=mag_x[:, c:c + 1])\
                    .then_inc(mag_x_ready, 1)

            def split_ks_t(c):
                cols = slice(c * STEP, (c + 1) * STEP)
                nc.scalar.activation(kt_hi[:, cols], ks_t_raw[:, cols], ACT.Copy, scale=scale_k)\
                    .then_inc(kt_hi_ready, 1)

            def split_ks(c):
                rows = slice(c * STEP // P, (c + 1) * STEP // P)
                act.wait_ge(ks_loaded[c % KS_SLOTS], 16 * (c // KS_SLOTS + 1))
                nc.scalar.activation(k_parts[:, rows, HIGH:WIDE], ks_raw[:, c % KS_SLOTS, :, :], ACT.Copy,
                                     scale=scale_k).then_inc(k_hi_ready, 1)

            for c in range(0, STEPS, 2):
                bound_x(c)
                if c == 0:
                    act.wait_ge(scale_step, 4)
                if c // 2 < EARLY:
                    split_ks_t(c // 2)
            act.wait_ge(scale_step, SCALE_STEPS)

            def make_rise(t, n):
                act.wait_ge(scores_ready, HALVES * t + n + 1)
                nc.scalar.activation(rise[:, n % BANKS, :], scores[:, n % BANKS, :], ACT.Relu, scale=RISE)\
                    .then_inc(rise_ready, 1)

            def exponentials(t, odd, e):
                cols = slice(e * PIECE, (e + 1) * PIECE)
                act.wait_ge(exp_bias_ready, t + 1)
                nc.scalar.activation(leaky[:, odd, cols], leaky[:, odd, cols], ACT.Exp,
                                     bias=exp_bias[:, odd:odd + 1], scale=slope_scale[:, 0:1])\
                    .then_inc(probs_ready, 1)

            def high_part(t, q):
                n = HALVES * t + q
                act.wait_ge(probs_t_ready, n + 1)
                wait(act, weighted_ready, n + 1 - PT_SLOTS)
                nc.scalar.activation(pt_hi[:, q % PT_SLOTS, :], probs_t[:, q % 2, :], ACT.Copy)\
                    .then_inc(pt_hi_ready, 1)

            def squares_of(t, odd):
                act.wait_ge(norm_step, NORM_STEPS * t + 1)
                nc.scalar.activation(squares[:, :], y[:, odd, :], ACT.Square, bias=neg_mean[:, :],
                                     accum_out=square_sum[:, :]).then_inc(norm_step, 1)

            def normalise(t, odd):
                act.wait_ge(norm_step, NORM_STEPS * t + 5)
                wait(act, out_stored[odd], 8 * (t - odd))
                nc.scalar.activation(normed[:, odd, :], y[:, odd, :], ACT.Identity, bias=shift[:, :],
                                     scale=rstd[:, :]).then_inc(norm_step, 1)

            def one_round(i, odd, peeled):
                for slot in range(HALVES):
                    for c, back in in_slot(slot, AT_SPLIT_KS_T, 2, STEPS - EARLY):
                        if peeled == back == 0:
                            split_ks_t(EARLY + c)
                    for c, back in in_slot(slot, AT_SPLIT_KS, 2, STEPS):
                        if peeled == back:
                            split_ks(c)
                    for _, back in in_slot(slot, AT_FINISH + 2, 1, 1):
                        if exists(peeled, back):
                            squares_of(i - back, (odd + back) % 2)
                    for _, back in in_slot(slot, AT_FINISH + 5, 1, 1):
                        if exists(peeled, back):
                            normalise(i - back, (odd + back) % 2)
                    for q, back in in_slot(slot, AT_HIGH, 1, HALVES):
                        if exists(peeled, back):
                            high_part(i - back, q)
                    for n, back in in_slot(slot, AT_RISE, 1, HALVES):
                        if exists(peeled, back):
                            make_rise(i - back, n)
                    for e, back in in_slot(slot, AT_EXP, PIECE // HALF, PIECES):
                        if exists(peeled, back):
                            exponentials(i - back, (odd + back) % 2, e)

            rounds(act, one_round)

        @block.vector
        def _(dve):
            def magnitude(to, raw):
                nc.vector.tensor_reduce(to, raw, AX.X, ALU.max, apply_absolute_value=True).then_inc(mag_step, 1)

            def power(column, n):
                one = slice(column, column + 1)
                dve.wait_ge(mag_all_ready, n + 1)
                nc.vector.tensor_scalar(expo[:, one], mag_all[:, one].bitcast(I32), EXP_MASK, None, ALU.bitwise_and)\
                    .then_inc(scale_step, 1)
                dve.wait_ge(scale_step, 4 * n + 1)
                nc.vector.tensor_scalar(expo[:, one], expo[:, one], float(MIN_EXP * MANT), None, ALU.max)\
                    .then_inc(scale_step, 1)
                dve.wait_ge(scale_step, 4 * n + 2)
                nc.vector.tensor_scalar(scale[:, one], expo[:, one], -1.0, float((254 + TOP) * MANT), ALU.mult, ALU.add)\
                    .then_inc(scale_step, 1)
                nc.vector.tensor_scalar(unscale[:, one], expo[:, one], -float(TOP * MANT), None, ALU.add)\
                    .then_inc(scale_step, 1)

            def split_ks_t(c):
                cols = slice(c * STEP, (c + 1) * STEP)
                dve.wait_ge(kt_hi_ready, c + 1)
                nc.vector.scalar_tensor_tensor(kt_lo[:, cols], ks_t_raw[:, cols], scale_k, kt_hi[:, cols],
                                               ALU.mult, ALU.subtract).then_inc(kt_lo_ready, 1)

            def split_ks(c):
                rows = slice(c * STEP // P, (c + 1) * STEP // P)
                dve.wait_ge(k_hi_ready, c + 1)
                nc.vector.scalar_tensor_tensor(k_parts[:, rows, LOW:D], ks_raw[:, c % KS_SLOTS, :, :], scale_k,
                                               k_parts[:, rows, HIGH:WIDE], ALU.mult, ALU.subtract)\
                    .then_inc(k_lo_ready, 1)

            for c in range(STEPS):
                dve.wait_ge(ks_t_loaded[c], 16)
                magnitude(mag_k[:, c:c + 1], ks_t_raw[:, c * STEP:(c + 1) * STEP])
            dve.wait_ge(mag_step, STEPS)
            magnitude(mag[:, 1:2], mag_k[:, :])
            power(1, 0)
            dve.wait_ge(scale_step, 4)
            for c in range(1, STEPS, 2):
                if c // 2 < EARLY:
                    split_ks_t(c // 2)
                dve.wait_ge(x_t_loaded[c], 16)
                magnitude(mag_x[:, c:c + 1], x_t_raw[:, c * STEP:(c + 1) * STEP])
            dve.wait_ge(mag_step, MAG_STEPS - 1)
            dve.wait_ge(mag_x_ready, STEPS // 2)
            magnitude(mag[:, 0:1], mag_x[:, :])
            power(0, 1)
            dve.wait_ge(scale_step, 8)
            nc.vector.tensor_scalar(slope_scale[:, 0:1], unscale_x, unscale_k, SLOPE, ALU.mult, ALU.mult)\
                .then_inc(scale_step, 1)
            dve.wait_ge(scale_step, 9)
            nc.vector.tensor_scalar(slope_scale[:, 1:2], slope_scale[:, 0:1], -1.0, None, ALU.mult)\
                .then_inc(scale_step, 1)

            def make_bias(t, c):
                j, at = c * STEP // LOAD, c * STEP % LOAD
                if at == 0:
                    dve.wait_ge(adj_loaded[j], 16 * (t + 1))
                wait(dve, masked_ready, HALVES * t + 2 * (c - BIASES + 1))
                nc.vector.tensor_scalar(bias[:, c % BIASES, :], adj_sb[:, j, at:at + STEP], 0.0, MASKED,
                                        ALU.is_le, ALU.mult).then_inc(bias_ready, 1)

            def make_leaky(t, odd, n, peeled):
                cols = slice(n * HALF, (n + 1) * HALF)
                dve.wait_ge(masked_ready, HALVES * t + n + 1)
                wait(dve, probs_t_ready, HALVES * (t - 2) + n + 1)
                if n == 0:
                    wait(dve, exp_bias_ready, t - 1)
                    first = -3.0e38
                else:
                    dve.wait_ge(leaky_ready, HALVES * t + n)
                    first = row_max[:, odd, n - 1:n]
                if peeled is not None and t == 0:
                    dve.wait_ge(kt_lo_ready, n // 2 + 1)
                detach(dve)
                nc.vector.tensor_tensor_reduce(leaky[:, odd, cols], scores[:, n % BANKS, :], rise[:, n % BANKS, :],
                                               1.0, first, ALU.add, ALU.max, row_max[:, odd, n:n + 1])\
                    .then_inc(leaky_ready, 1)

            def make_exp_bias(t, odd):
                dve.wait_ge(leaky_ready, HALVES * (t + 1))
                wait(dve, probs_ready, PIECES * (t - 1))
                nc.vector.tensor_scalar(exp_bias[:, odd:odd + 1], row_max[:, odd, HALVES - 1:HALVES],
                                        slope_scale[:, 1:2], PROB_LIFT, ALU.mult, ALU.add)\
                    .then_inc(exp_bias_ready, 1)

            def low_part(t, q):
                n = HALVES * t + q
                dve.wait_ge(pt_hi_ready, n + 1)
                nc.vector.tensor_tensor(pt_lo[:, q % PT_SLOTS, :], probs_t[:, q % 2, :],
                                        pt_hi[:, q % PT_SLOTS, :], ALU.subtract).then_inc(pt_lo_ready, 1)

            def finish(t, odd):
                dve.wait_ge(weighted_ready, HALVES * (t + 1))
                nc.vector.tensor_scalar(denom[:, :], weighted[:, odd, ONES:ONES + 1], scale_k, None, ALU.mult)\
                    .then_inc(final_step, 1)
                dve.wait_ge(final_step, 4 * t + 1)
                nc.vector.reciprocal(recip[:, :], denom[:, :]).then_inc(final_step, 1)
                dve.wait_ge(xrow_loaded[odd], 8 * (t - odd) + 16)
                dve.wait_ge(final_step, 4 * t + 2)
                nc.vector.scalar_tensor_tensor(y0[:, :], weighted[:, odd, LOW:D], recip[:, :], x_row[:, odd, :],
                                               ALU.mult, ALU.add).then_inc(final_step, 1)
                dve.wait_ge(final_step, 4 * t + 3)
                wait(dve, norm_step, NORM_STEPS * (t - 1))
                nc.vector.scalar_tensor_tensor(y[:, odd, :], weighted[:, odd, HIGH:WIDE], recip[:, :], y0[:, :],
                                               ALU.mult, ALU.add, accum_out=y_sum[:, odd:odd + 1])\
                    .then_inc(final_step, 1)

            def one_round(i, odd, peeled):
                for slot in range(HALVES):
                    for c, back in in_slot(slot, AT_BIAS, 2, STEPS):
                        if exists(peeled, back):
                            make_bias(i - back, c)
                    for c, back in in_slot(slot, AT_SPLIT_KS_T, 2, STEPS - EARLY):
                        if peeled == back == 0:
                            split_ks_t(EARLY + c)
                    for c, back in in_slot(slot, AT_SPLIT_KS, 2, STEPS):
                        if peeled == back:
                            split_ks(c)
                    for n, back in in_slot(slot, AT_LEAKY, 1, HALVES):
                        if exists(peeled, back):
                            make_leaky(i - back, (odd + back) % 2, n, peeled)
                            if n == HALVES - 1:
                                make_exp_bias(i - back, (odd + back) % 2)
                    for q, back in in_slot(slot, AT_LOW, 1, HALVES):
                        if exists(peeled, back):
                            low_part(i - back, q)
                    for _, back in in_slot(slot, AT_FINISH, 1, 1):
                        if exists(peeled, back):
                            finish(i - back, (odd + back) % 2)

            rounds(dve, one_round)

        @block.tensor
        def _(pe):
            pe.wait_ge(const_step, 5)

            def score(t, odd, n, peeled):
                c, cols = n // 2, slice(n * HALF, (n + 1) * HALF)
                to = scores[:, n % BANKS, :]
                wait(pe, leaky_ready, HALVES * t + n + 1 - BANKS)
                if n == 0:
                    pe.wait_ge(xt_step, 3 * t + 3)
                if peeled is not None:
                    pe.wait_ge(kt_lo_ready, min(STEPS, STEPS * t + c + 1))
                nc.tensor.matmul(to, xt_hi[:, odd, :], kt_hi[:, cols], start=True, stop=False)
                nc.tensor.matmul(to, xt_hi[:, odd, :], kt_lo[:, cols], start=False, stop=False)
                nc.tensor.matmul(to, xt_lo[:, odd, :], kt_hi[:, cols], start=False, stop=True)\
                    .then_inc(scores_ready, 1)

            def transpose(t, odd, q):
                n = HALVES * t + q
                if q * HALF % PIECE == 0:
                    pe.wait_ge(probs_ready, PIECES * t + q * HALF // PIECE + 1)
                wait(pe, pt_lo_ready, n - 1)
                for b in range(BLOCKS):
                    at = q * HALF + b * P
                    last = nc.tensor.transpose(probs_t[:, q % 2, b * P:(b + 1) * P],
                                               leaky[:, odd, at:at + P], eye[:, :])
                last.then_inc(probs_t_ready, 1)

            def weigh(t, odd, q, peeled):
                slot = q % PT_SLOTS
                pe.wait_ge(pt_lo_ready, HALVES * t + q + 1)
                if q == 0:
                    wait(pe, final_step, 4 * (t - 1))
                if peeled is not None:
                    pe.wait_ge(k_lo_ready, STEPS if t else q // 2 + 1)
                for b in range(BLOCKS):
                    rows = q * BLOCKS + b
                    cols = slice(b * P, (b + 1) * P)
                    nc.tensor.matmul(weighted[:, odd, 0:WIDE], pt_hi[:, slot, cols], k_parts[:, rows, :],
                                     start=(rows == 0), stop=False, skip_group_check=True)
                    last = nc.tensor.matmul(weighted[:, odd, ONES:WIDE], pt_lo[:, slot, cols],
                                            k_parts[:, rows, ONES:WIDE], start=False,
                                            stop=(rows == M // P - 1), skip_group_check=True)
                last.then_inc(weighted_ready, 1)

            def one_round(i, odd, peeled):
                for slot in range(HALVES):
                    for n, back in in_slot(slot, AT_SCORE, 1, HALVES):
                        if exists(peeled, back):
                            score(i - back, (odd + back) % 2, n, peeled)
                    for q, back in in_slot(slot, AT_TRANSPOSE, 1, HALVES):
                        if exists(peeled, back):
                            transpose(i - back, (odd + back) % 2, q)
                    for q, back in in_slot(slot, AT_WEIGH, 1, HALVES):
                        if exists(peeled, back):
                            weigh(i - back, (odd + back) % 2, q, peeled)

            rounds(pe, one_round)


def kernel(x, adj, L0_gnn_ks):
    import numpy as np
    import concourse.bacc as bacc
    from concourse.bass_utils import run_bass_kernel_spmd

    x, adj, ks = np.asarray(x), np.asarray(adj), np.asarray(L0_gnn_ks)
    arrays = {
        "in_x": np.ascontiguousarray(x),
        "in_x_t": np.ascontiguousarray(x.T),
        "in_ks": np.ascontiguousarray(ks),
        "in_ks_t": np.ascontiguousarray(ks.T),
        "in_adj": np.ascontiguousarray(adj),
    }
    nc = bacc.Bacc("TRN2", target_bir_lowering=False, num_devices=1)
    args = [nc.dram_tensor(name, a.shape, mybir.dt.from_np(a.dtype), kind="ExternalInput").ap()
            for name, a in arrays.items()]
    out = nc.dram_tensor("out_0", x.shape, mybir.dt.float32, kind="ExternalOutput").ap()
    adj_attention_layernorm(nc, *args, out)
    r = run_bass_kernel_spmd(nc, [arrays], core_ids=[0])
    return r.results[0]["out_0"]
```
